# Optimizing a Trainium2 kernel written in Bass

```python
import numpy as np
import jax
import jax.numpy as jnp

def _softmax(x, axis=-1):
    return jax.nn.softmax(x, axis=axis)

def _gelu(x):
    return jax.nn.gelu(x, approximate=True)

def _silu(x):
    return jax.nn.silu(x)

def _sigmoid(x):
    return jax.nn.sigmoid(x)

def _layernorm(x, axis=-1, eps=1e-05):
    m = jnp.mean(x, axis=axis, keepdims=True)
    v = jnp.var(x, axis=axis, keepdims=True)
    return (x - m) / jnp.sqrt(v + eps)

def _scatter_add(tgt, idx, src, axis=0):
    return tgt.at[idx].add(src)

def _segment_sum(src, seg, n):
    return jax.ops.segment_sum(src, seg, n)
kernel_name = 'mk_rec_standalone_d1_rec_r8_6effc5'

def setup_inputs(seed: int=0):
    np.random.seed(seed)
    _w = jnp.asarray

    def _rec_inputs():
        import jax
        import jax.numpy as jnp
        _rk = jax.random.key(seed)
        r_x1 = jax.random.randint(jax.random.fold_in(_rk, 1), (512,), 0, 512, jnp.int32)
        r_x2 = jax.random.randint(jax.random.fold_in(_rk, 2), (512,), 0, 512, jnp.int32)
        return (r_x1, r_x2)
    r_x1, r_x2 = _rec_inputs()

    def _L0_rec_setup():
        import jax, jax.numpy as jnp
        import numpy as np
        DIM_D = 512
        ALPHA = 1.0
        BATCH = 131072
        key = jax.random.key(seed)
        k1, k2, k3, k4 = jax.random.split(key, 4)
        U = ALPHA * jnp.eye(DIM_D, dtype=jnp.float32) + 0.01 * jax.random.normal(k1, (DIM_D, DIM_D), dtype=jnp.float32)
        V = ALPHA * jnp.eye(DIM_D, dtype=jnp.float32) + 0.01 * jax.random.normal(k2, (DIM_D, DIM_D), dtype=jnp.float32)
        x1 = jax.random.randint(k3, (BATCH,), 0, DIM_D, dtype=jnp.int64 if jax.config.jax_enable_x64 else jnp.int32)
        x2 = jax.random.randint(k4, (BATCH,), 0, DIM_D, dtype=jnp.int64 if jax.config.jax_enable_x64 else jnp.int32)
        return {'U': U, 'V': V, 'x1': x1, 'x2': x2}
    _L0_rec_all = _L0_rec_setup()
    _L0_rec_in = {k: v for k, v in _L0_rec_all.items() if k in ('U', 'V')}
    del _L0_rec_all
    return {'r_x1': r_x1, 'r_x2': r_x2, 'L0_rec_U': _L0_rec_in['U'], 'L0_rec_V': _L0_rec_in['V']}

def reference(r_x1, r_x2, L0_rec_U, L0_rec_V):
    import jax
    import jax.numpy as jnp

    def _L0_rec_ref(U, V, x1, x2):
        import jax, jax.numpy as jnp
        import numpy as np
        DIM_D = 512
        ALPHA = 1.0
        BATCH = 131072
        M = U @ U.T - V @ V.T
        return M[x1, x2]
    y = _L0_rec_ref(L0_rec_U, L0_rec_V, r_x1, r_x2)
    return y

_drawn_inputs = setup_inputs


def setup_inputs(seed=0):
    import zlib

    import numpy as np

    out = dict(_drawn_inputs(seed))
    spreads = {}
    factors = {}
    for name, (base, spread) in spreads.items():
        noise = np.random.default_rng([zlib.crc32(name.encode()), seed]).standard_normal(out[name].shape)
        drawn = base * np.exp(spread * noise) if base else spread * noise
        out[name] = jnp.asarray(drawn.astype(out[name].dtype))
    for name, factor in factors.items():
        out[name] = (out[name] * factor).astype(out[name].dtype)
    return out
```

```python
from contextlib import ExitStack

import concourse.bass as bass
from concourse import mybir

P = 128
ALU = mybir.AluOpType
F32 = mybir.dt.float32
I32 = mybir.dt.int32


def gathered_gram_difference(nc, x1, x2, uv, y):
    (batch,) = x1.shape
    _, width = uv.shape
    dim = width // 2
    groups = batch // P

    x1_dram = x1.rearrange("(p g) -> p g", g=groups)
    x2_dram = x2.rearrange("(p g) -> p g", g=groups)
    y_dram = y.rearrange("(p g) -> p g", g=groups)

    with ExitStack() as ctx:
        def sb(name, shape, dt):
            return ctx.enter_context(nc.sbuf_tensor(name, shape, dt))

        def sem(name):
            return ctx.enter_context(nc.semaphore(name))

        idx1 = sb("idx1", [P, groups], I32)
        idx2 = sb("idx2", [P, groups], I32)
        rows1 = sb("rows1", [P, groups, width], F32)
        rows2 = sb("rows2", [P, groups, width], F32)
        u_dot = sb("u_dot", [P, groups], F32)
        y_sb = sb("y_sb", [P, groups], F32)

        idx1_loaded = sem("idx1_loaded")
        idx2_loaded = sem("idx2_loaded")
        rows1_loaded = [sem(f"rows1_loaded{g}") for g in range(groups)]
        rows2_loaded = [sem(f"rows2_loaded{g}") for g in range(groups)]
        u_dots = sem("u_dots")
        y_ready = sem("y_ready")
        y_stored = sem("y_stored")

        block = ctx.enter_context(nc.Block())

        @block.sync
        def _(sp):
            sp.dma_start(idx1[:], x1_dram).then_inc(idx1_loaded, 16)
            sp.wait_ge(y_ready, groups)
            sp.dma_start(y_dram, y_sb[:]).then_inc(y_stored, 16)
            sp.wait_ge(y_stored, 16)

        @block.scalar
        def _(act):
            act.dma_start(idx2[:], x2_dram).then_inc(idx2_loaded, 16)

        @block.gpsimd
        def _(pool):
            pool.wait_ge(idx1_loaded, 16)
            for g in range(groups):
                pool.indirect_dma_start(rows1[:, g, :], None, uv,
                                        bass.IndirectOffsetOnAxis(idx1[:, g:g + 1], 0)
                                        ).then_inc(rows1_loaded[g], 16)
                if g == 0:
                    pool.wait_ge(idx2_loaded, 16)
                pool.indirect_dma_start(rows2[:, g, :], None, uv,
                                        bass.IndirectOffsetOnAxis(idx2[:, g:g + 1], 0)
                                        ).then_inc(rows2_loaded[g], 16)

        @block.vector
        def _(dve):
            for g in range(groups):
                dve.wait_ge(rows1_loaded[g], 16)
                dve.wait_ge(rows2_loaded[g], 16)
                dve.tensor_tensor_reduce(rows1[:, g, 0:dim], rows1[:, g, 0:dim], rows2[:, g, 0:dim],
                                         1.0, 0.0, ALU.mult, ALU.add, u_dot[:, g:g + 1]).then_inc(u_dots, 1)
                dve.wait_ge(u_dots, g + 1)
                dve.tensor_tensor_reduce(rows1[:, g, dim:], rows1[:, g, dim:], rows2[:, g, dim:],
                                         -1.0, u_dot[:, g:g + 1], ALU.mult, ALU.add,
                                         y_sb[:, g:g + 1]).then_inc(y_ready, 1)


def kernel(r_x1, r_x2, L0_rec_U, L0_rec_V):
    import numpy as np
    import concourse.bacc as bacc
    from concourse.bass_utils import run_bass_kernel_spmd

    nc = bacc.Bacc("TRN2", target_bir_lowering=False, num_devices=1)
    arrays = {
        "x1": np.ascontiguousarray(r_x1),
        "x2": np.ascontiguousarray(r_x2),
        "uv": np.ascontiguousarray(np.concatenate([np.asarray(L0_rec_U), np.asarray(L0_rec_V)], axis=1)),
    }
    aps = [nc.dram_tensor(name, a.shape, mybir.dt.from_np(a.dtype), kind="ExternalInput").ap()
           for name, a in arrays.items()]
    y = nc.dram_tensor("y", arrays["x1"].shape, F32, kind="ExternalOutput").ap()
    gathered_gram_difference(nc, *aps, y)
    result = run_bass_kernel_spmd(nc, [arrays], core_ids=[0])
    return result.results[0]["y"]
```

```python
from contextlib import ExitStack

import concourse.bass as bass
from concourse import mybir

P = 128
BANK = 512
ALU = mybir.AluOpType
ACT = mybir.ActivationFunctionType
F32 = mybir.dt.float32
F32R = mybir.dt.float32r
F16 = mybir.dt.float16
BF16 = mybir.dt.bfloat16
I32 = mybir.dt.int32

HEAD_BLOCKS = 2
HEAD_FROM = 1
WARM_BEFORE_INDICES = 6 * [BANK] + [256]
WARM_BEFORE_MASKS = [BANK]
DVE_MASKS = [(0, 0), (0, 1), (0, 2), (0, 3), (1, 3)]
ACT_CHUNKS = [0, 1, 2]
MASK_ORDER = [(0, 0), (0, 1), (1, 0), (0, 2), (1, 1), (0, 3), (1, 2), (1, 3)]


def gathered_gram_difference(nc, x, uv, y):
    sides, batch = x.shape
    rows, width = uv.shape
    dim = width // 2
    groups = batch // P
    chunks = rows // P
    blocks = HEAD_BLOCKS
    head_width = blocks * P
    head_batch = batch - HEAD_FROM * P
    tail_from = [0 if g < HEAD_FROM else head_width for g in range(groups)]
    assert sides == 2 and rows == chunks * P and batch == groups * P and batch <= 512

    idx_dram = x.rearrange("s (p g) -> p s g", g=groups)
    y_dram = y.rearrange("(p g) -> p g", g=groups)
    head_dram = uv[:, 0:head_width].rearrange("(k p) c -> p k c", p=P)
    half = chunks // 2

    with ExitStack() as ctx:
        def sb(name, shape, dt):
            return ctx.enter_context(nc.sbuf_tensor(name, shape, dt))

        def psum(name, shape, dt):
            return ctx.enter_context(nc.psum_tensor(name, shape, dt))

        def sem(name):
            return ctx.enter_context(nc.semaphore(name))

        idx = sb("idx", [P, sides, groups], I32)
        idx_row = sb("idx_row", [sides, batch], I32)
        idx_row16 = sb("idx_row16", [sides, groups - HEAD_FROM, P], F16)
        pick_side = sb("pick_side", [sides, sides, P], F16)
        row_id = sb("row_id", [P, chunks], F32)
        neg_row_id = sb("neg_row_id", [P, chunks], F32)
        zeros = sb("zeros", [P, BANK], BF16)
        ones = sb("ones", [P, 1], F32)

        head = sb("head", [P, chunks, head_width], F32)
        head_hi = sb("head_hi", [P, chunks, head_width], F32R)
        head_lo = sb("head_lo", [P, chunks, head_width], F32R)
        mask = sb("mask", [P, sides, chunks, head_batch], F32R)
        distance = sb("distance", [P, len(ACT_CHUNKS), head_batch], F32)
        picked1 = sb("picked1", [P, blocks, head_batch], F32)
        head_prod = sb("head_prod", [P, blocks, head_batch], F32)

        rows_of = [sb(f"rows_of{s}", [P, groups, width], F32) for s in range(sides)]
        u_dot = sb("u_dot", [P, groups], F32)
        tail_dot = sb("tail_dot", [P, groups], F32)
        y_sb = sb("y_sb", [P, groups], F32)

        ps_idx = psum("ps_idx", [P, sides + 1, BANK], F32)
        ps_pick = psum("ps_pick", [P, sides, blocks, BANK], F32)
        ps_dot = psum("ps_dot", [P, BANK], F32)

        idx_loaded = sem("idx_loaded")
        idx_row_loaded = sem("idx_row_loaded")
        head_loaded = [sem(f"head_loaded{h}") for h in range(2)]
        tail_loaded = [[sem(f"tail_loaded{s}_{g}") for g in range(groups)] for s in range(sides)]
        last_v_loaded = sem("last_v_loaded")
        zeros_set = sem("zeros_set")
        ones_set = sem("ones_set")
        side_ones_set = sem("side_ones_set")
        pick_side_set = sem("pick_side_set")
        row_id_set = sem("row_id_set")
        neg_row_id_set = sem("neg_row_id_set")
        idx_row16_set = sem("idx_row16_set")
        idx_spread = sem("idx_spread")
        hi_ready = sem("hi_ready")
        lo_ready = sem("lo_ready")
        dve_masks = sem("dve_masks")
        distances = sem("distances")
        act_masks = sem("act_masks")
        picked = [sem(f"picked{s}") for s in range(sides)]
        picked1_copied = sem("picked1_copied")
        head_prods = sem("head_prods")
        head_summed = sem("head_summed")
        u_dots = sem("u_dots")
        tail_dots = sem("tail_dots")
        y_ready = sem("y_ready")
        y_stored = sem("y_stored")

        block = ctx.enter_context(nc.Block())
        last = groups - 1

        @block.sync
        def _(sp):
            sp.dma_start(idx[:], idx_dram).then_inc(idx_loaded, 16)
            for h in range(2):
                sp.dma_start(head[:, h * half:(h + 1) * half, :],
                             head_dram[:, h * half:(h + 1) * half, :]).then_inc(head_loaded[h], 16)
            sp.wait_ge(y_ready, 1)
            sp.dma_start(y_dram, y_sb[:]).then_inc(y_stored, 16)
            sp.wait_ge(y_stored, 16)

        @block.gpsimd
        def _(pool):
            pool.iota(row_id[:], [[P, chunks]], base=0, channel_multiplier=1,
                      allow_small_or_imprecise_dtypes=True).then_inc(row_id_set, 1)
            pool.iota(neg_row_id[:], [[-P, chunks]], base=0, channel_multiplier=-1,
                      allow_small_or_imprecise_dtypes=True).then_inc(neg_row_id_set, 1)
            pool.memset(pick_side[:], 1.0).then_inc(side_ones_set, 1)
            pool.wait_ge(side_ones_set, 1)
            pool.affine_select(out=pick_side[:], in_=pick_side[:], compare_op=ALU.is_equal, fill=0.0,
                               base=0, pattern=[[-1, sides], [0, P]],
                               channel_multiplier=1).then_inc(pick_side_set, 1)
            pool.wait_ge(idx_loaded, 16)

            def gather(side, g, first, end, loaded):
                pool.indirect_dma_start(rows_of[side][:, g, first:end], None, uv,
                                        bass.IndirectOffsetOnAxis(idx[:, side, g:g + 1], 0),
                                        element_offset=first).then_inc(loaded, 16)

            for g in range(last):
                gather(0, g, tail_from[g], width, tail_loaded[0][g])
                gather(1, g, tail_from[g], width, tail_loaded[1][g])
            gather(0, last, tail_from[last], width, tail_loaded[0][last])
            gather(1, last, tail_from[last], dim, tail_loaded[1][last])
            gather(1, last, dim, width, last_v_loaded)

        @block.scalar
        def _(act):
            act.dma_start(idx_row[:], x).then_inc(idx_row_loaded, 16)
            act.wait_ge(idx_row_loaded, 16)
            act.copy(idx_row16[:], idx_row[:].rearrange("s (p g) -> s g p", g=groups)[:, HEAD_FROM:, :]
                     ).then_inc(idx_row16_set, 1)

            def split_hi(h):
                act.wait_ge(head_loaded[h], 16)
                act.copy(head_hi[:, h * half:(h + 1) * half, :],
                         head[:, h * half:(h + 1) * half, :]).then_inc(hi_ready, 1)

            def build_mask(n):
                k = ACT_CHUNKS[n]
                act.wait_ge(idx_spread, sides + 1)
                act.wait_ge(neg_row_id_set, 1)
                act.activation(distance[:, n, :], ps_idx[:, sides, 0:head_batch], ACT.Abs,
                               bias=neg_row_id[:, k:k + 1]).then_inc(distances, 1)
                act.wait_ge(distances, n + 1)
                act.activation(mask[:, 1, k, :], distance[:, n, :], ACT.Relu,
                               bias=1.0, scale=-1.0).then_inc(act_masks, 1)

            split_hi(0)
            split_hi(1)
            for n in range(len(ACT_CHUNKS)):
                build_mask(n)
            for b in range(blocks):
                act.wait_ge(picked[0], b + 1)
                act.copy(picked1[:, b, :], ps_pick[:, 0, b, 0:head_batch]).then_inc(picked1_copied, 1)

        @block.tensor
        def _(pe):
            def warm(widths):
                for width_ in widths:
                    pe.matmul(ps_dot[:, 0:width_], zeros[:, 0:P], zeros[:, 0:width_], start=True, stop=True)

            def pick(side, k, part, b):
                return pe.matmul(ps_pick[:, side, b, 0:head_batch], part[:, k, b * P:(b + 1) * P],
                                 mask[:, side, k, :], start=(k == 0 and part is head_hi),
                                 stop=(k == chunks - 1 and part is head_lo))

            def sum_columns(b):
                pe.wait_ge(head_prods, b + 1)
                for g in range(HEAD_FROM, groups):
                    at = (g - HEAD_FROM) * P
                    summing = pe.matmul(ps_dot[:, g:g + 1], head_prod[:, b, at:at + P], ones[:],
                                        start=(b == 0 and g == HEAD_FROM), stop=(b == blocks - 1),
                                        skip_group_check=True)
                return summing

            pe.wait_ge(zeros_set, 1)
            warm(WARM_BEFORE_INDICES)
            pe.wait_ge(pick_side_set, 1)
            pe.wait_ge(idx_row16_set, 1)
            for bank, side in enumerate((0, 1, 1)):
                pe.matmul(ps_idx[:, bank, 0:head_batch], pick_side[:, side, :],
                          idx_row16[:].rearrange("s g p -> s (g p)"),
                          start=True, stop=True).then_inc(idx_spread, 1)
            warm(WARM_BEFORE_MASKS)
            for side, k in MASK_ORDER:
                if side == 1 and k in ACT_CHUNKS:
                    pe.wait_ge(act_masks, ACT_CHUNKS.index(k) + 1)
                else:
                    pe.wait_ge(dve_masks, DVE_MASKS.index((side, k)) + 1)
                for part, split in ((head_hi, hi_ready), (head_lo, lo_ready)):
                    pe.wait_ge(split, k // half + 1)
                    picking = pick(side, k, part, 0)
                if k == chunks - 1:
                    picking.then_inc(picked[side], 1)
            for b in range(1, blocks):
                for side in range(sides):
                    for k in range(chunks):
                        for part in (head_hi, head_lo):
                            picking = pick(side, k, part, b)
                    picking.then_inc(picked[side], 1)
            pe.wait_ge(ones_set, 1)
            for b in range(blocks):
                summing = sum_columns(b)
            summing.then_inc(head_summed, 1)

        @block.vector
        def _(dve):
            dve.memset(zeros[:], 0.0).then_inc(zeros_set, 1)
            dve.memset(ones[:], 1.0).then_inc(ones_set, 1)

            def build_mask(side, k):
                dve.wait_ge(idx_spread, side + 1)
                dve.tensor_scalar(mask[:, side, k, :], ps_idx[:, side, 0:head_batch], row_id[:, k:k + 1],
                                  None, ALU.is_equal).then_inc(dve_masks, 1)

            def split_lo(h):
                dve.wait_ge(hi_ready, h + 1)
                part = slice(h * half, (h + 1) * half)
                dve.tensor_tensor(head_lo[:, part, :], head[:, part, :], head_hi[:, part, :].bitcast(F32),
                                  ALU.subtract).then_inc(lo_ready, 1)

            def tail_product(g, first, end, sign, start, out):
                row1, row2 = (gathered[:, g, first:end] for gathered in rows_of)
                return dve.tensor_tensor_reduce(row1, row1, row2, sign, start, ALU.mult, ALU.add, out)

            def u_part(g):
                dve.wait_ge(tail_loaded[0][g], 16)
                dve.wait_ge(tail_loaded[1][g], 16)
                tail_product(g, tail_from[g], dim, 1.0, 0.0, u_dot[:, g:g + 1]).then_inc(u_dots, 1)

            def v_part(g):
                if g == last:
                    dve.wait_ge(last_v_loaded, 16)
                dve.wait_ge(u_dots, g + 1)
                out = y_sb if g < HEAD_FROM else tail_dot
                tail_product(g, dim, width, -1.0, u_dot[:, g:g + 1],
                             out[:, g:g + 1]).then_inc(tail_dots, 1)

            def multiply_heads(b):
                dve.wait_ge(picked[1], b + 1)
                dve.wait_ge(picked1_copied, b + 1)
                dve.tensor_tensor(head_prod[:, b, :], picked1[:, b, :], ps_pick[:, 1, b, 0:head_batch],
                                  ALU.mult).then_inc(head_prods, 1)

            dve.wait_ge(row_id_set, 1)
            for n, (side, k) in enumerate(DVE_MASKS):
                build_mask(side, k)
                if n % half == 0 and n < chunks:
                    split_lo(n // half)
            for g in range(last):
                u_part(g)
                v_part(g)
                if g == last - 2:
                    multiply_heads(0)
            for b in range(1, blocks):
                multiply_heads(b)
            u_part(last)
            v_part(last)
            dve.wait_ge(head_summed, 1)
            dve.wait_ge(tail_dots, groups)
            dve.tensor_tensor(y_sb[:, HEAD_FROM:], tail_dot[:, HEAD_FROM:],
                              ps_dot[:, HEAD_FROM:groups], ALU.add).then_inc(y_ready, 1)


def kernel(r_x1, r_x2, L0_rec_U, L0_rec_V):
    import numpy as np
    import concourse.bacc as bacc
    from concourse.bass_utils import run_bass_kernel_spmd

    nc = bacc.Bacc("TRN2", target_bir_lowering=False, num_devices=1)
    arrays = {
        "x": np.ascontiguousarray(np.stack([np.asarray(r_x1), np.asarray(r_x2)])),
        "uv": np.ascontiguousarray(np.concatenate([np.asarray(L0_rec_U), np.asarray(L0_rec_V)], axis=1)),
    }
    aps = [nc.dram_tensor(name, a.shape, mybir.dt.from_np(a.dtype), kind="ExternalInput").ap()
           for name, a in arrays.items()]
    y = nc.dram_tensor("y", arrays["x"].shape[1:], F32, kind="ExternalOutput").ap()
    gathered_gram_difference(nc, *aps, y)
    result = run_bass_kernel_spmd(nc, [arrays], core_ids=[0])
    return result.results[0]["y"]
```
